# Optimizing a Trainium2 kernel written in Bass

```python
import numpy as np
import jax
import jax.numpy as jnp

def _softmax(x, axis=-1):
    return jax.nn.softmax(x, axis=axis)

def _gelu(x):
    return jax.nn.gelu(x, approximate=True)

def _silu(x):
    return jax.nn.silu(x)

def _sigmoid(x):
    return jax.nn.sigmoid(x)

def _layernorm(x, axis=-1, eps=1e-05):
    m = jnp.mean(x, axis=axis, keepdims=True)
    v = jnp.var(x, axis=axis, keepdims=True)
    return (x - m) / jnp.sqrt(v + eps)

def _scatter_add(tgt, idx, src, axis=0):
    return tgt.at[idx].add(src)

def _segment_sum(src, seg, n):
    return jax.ops.segment_sum(src, seg, n)
kernel_name = 'mk_rec_standalone_d1_rec_r8_0680d7'

def setup_inputs(seed: int=0):
    np.random.seed(seed)
    _w = jnp.asarray

    def _rec_inputs():
        import jax
        import jax.numpy as jnp
        _rk = jax.random.key(seed)
        r_x = -0.000154849 + 1.00019 * jax.random.normal(jax.random.fold_in(_rk, 1), (2048, 40, 64), jnp.float32)
        return r_x
    r_x = _rec_inputs()

    def _L0_rec_setup():
        import jax, jax.numpy as jnp
        import numpy as np
        N_FEATURE = 40
        EMBED_DIM = 64
        HIDDEN = 64
        OUT_DIM = 1
        BATCH = 256
        _ROW, _COL = np.triu_indices(N_FEATURE, k=1)
        ROW = jnp.asarray(_ROW)
        COL = jnp.asarray(_COL)
        key = jax.random.key(seed)
        ks = jax.random.split(key, 7)
        s_e = 1.0 / np.sqrt(EMBED_DIM)
        s_h = 1.0 / np.sqrt(HIDDEN)
        return {'x': jax.random.normal(ks[0], (BATCH, N_FEATURE, EMBED_DIM), jnp.float32), 'W1': jax.random.uniform(ks[1], (HIDDEN, EMBED_DIM), jnp.float32, -s_e, s_e), 'b1': jax.random.uniform(ks[2], (HIDDEN,), jnp.float32, -s_e, s_e), 'W2': jax.random.uniform(ks[3], (1, HIDDEN), jnp.float32, -s_h, s_h), 'b2': jax.random.uniform(ks[4], (1,), jnp.float32, -s_h, s_h), 'Wl': jax.random.uniform(ks[5], (OUT_DIM, EMBED_DIM), jnp.float32, -s_e, s_e), 'bl': jax.random.uniform(ks[6], (OUT_DIM,), jnp.float32, -s_e, s_e)}
    _L0_rec_all = _L0_rec_setup()
    _L0_rec_in = {k: v for k, v in _L0_rec_all.items() if k in ('W1', 'b1', 'W2', 'b2', 'Wl', 'bl')}
    del _L0_rec_all
    return {'r_x': r_x, 'L0_rec_W1': _L0_rec_in['W1'], 'L0_rec_b1': _L0_rec_in['b1'], 'L0_rec_W2': _L0_rec_in['W2'], 'L0_rec_b2': _L0_rec_in['b2'], 'L0_rec_Wl': _L0_rec_in['Wl'], 'L0_rec_bl': _L0_rec_in['bl']}

def reference(r_x, L0_rec_W1, L0_rec_b1, L0_rec_W2, L0_rec_b2, L0_rec_Wl, L0_rec_bl):
    import jax
    import jax.numpy as jnp

    def _L0_rec_ref(x, W1, b1, W2, b2, Wl, bl):
        import jax, jax.numpy as jnp
        import numpy as np
        N_FEATURE = 40
        EMBED_DIM = 64
        HIDDEN = 64
        OUT_DIM = 1
        BATCH = 256
        _ROW, _COL = np.triu_indices(N_FEATURE, k=1)
        ROW = jnp.asarray(_ROW)
        COL = jnp.asarray(_COL)
        p = x[:, ROW, :]
        q = x[:, COL, :]
        inner = p * q
        h = jax.nn.relu(jnp.einsum('bpe,he->bph', inner, W1) + b1)
        logits = jnp.einsum('bph,oh->bpo', h, W2) + b2
        attn = jax.nn.softmax(logits, axis=1)
        pooled = jnp.sum(inner * attn, axis=1)
        return pooled @ Wl.T + bl
    y = _L0_rec_ref(r_x, L0_rec_W1, L0_rec_b1, L0_rec_W2, L0_rec_b2, L0_rec_Wl, L0_rec_bl)
    return y

_drawn_inputs = setup_inputs


def setup_inputs(seed=0):
    import zlib

    import numpy as np

    out = dict(_drawn_inputs(seed))
    spreads = {}
    factors = {}
    for name, (base, spread) in spreads.items():
        noise = np.random.default_rng([zlib.crc32(name.encode()), seed]).standard_normal(out[name].shape)
        drawn = base * np.exp(spread * noise) if base else spread * noise
        out[name] = jnp.asarray(drawn.astype(out[name].dtype))
    for name, factor in factors.items():
        out[name] = (out[name] * factor).astype(out[name].dtype)
    return out
```

```python
from contextlib import ExitStack

import concourse.bass as bass
from concourse import mybir

F32 = mybir.dt.float32
ALU = mybir.AluOpType
ACT = mybir.ActivationFunctionType
AX_X = mybir.AxisListType.X

P = 128


def window_view(tile, offset, dims):
    whole = tile[:, :]
    return bass.AP(whole.tensor, whole.offset + offset, [list(whole.ap[0])] + dims)


def pair_attention_kernel(nc, x, w1, b1, w2, b2, wl, bl, y):
    BATCH, FIELDS, EMBED = x.shape
    HIDDEN = w1.shape[0]
    assert EMBED == HIDDEN == P // 2

    DUOS = BATCH // 2
    SHIFTS = FIELDS // 2 - 1
    LAST = FIELDS // 2
    PAIRS = SHIFTS * FIELDS + LAST
    HALF = PAIRS // 2
    EXT = FIELDS + LAST

    WINDOWS = 16
    STEP_DUOS = 2
    ROUND_DUOS = WINDOWS * STEP_DUOS
    ROUNDS = DUOS // ROUND_DUOS
    CHUNK_DUOS = 16
    CHUNK_STEPS = CHUNK_DUOS // STEP_DUOS
    CHUNKS_PER_ROUND = ROUND_DUOS // CHUNK_DUOS
    TT = CHUNK_DUOS * FIELDS // P
    U = FIELDS // TT
    RING = 4
    BANK = 512
    QUAD = 32
    MID = QUAD - 2
    assert P * TT == CHUNK_DUOS * FIELDS and U * TT == FIELDS and LAST % TT == 0

    with ExitStack() as ctx:
        def sb(name, shape, dt=F32):
            return ctx.enter_context(nc.sbuf_tensor(name, shape, dt))

        def pb(name, shape):
            return ctx.enter_context(nc.psum_tensor(name, shape, F32))

        def sem(name):
            return ctx.enter_context(nc.semaphore(name))

        ident = sb("ident", [P, P])
        w1_rows = sb("w1_rows", [P, P])
        w1_block = sb("w1_block", [P, P])
        w2_window = sb("w2_window", [P, MID + QUAD])
        wl_window = sb("wl_window", [P, MID + QUAD])
        b1_col = sb("b1_col", [P, 1])
        b2_col = sb("b2_col", [P, 1])
        bl_col = sb("bl_col", [P, 1])
        x_rows = [sb(f"x_rows{s}", [P, TT, 2, EMBED]) for s in range(2)]
        xt = [sb(f"xt{s}", [P, CHUNK_DUOS * EXT]) for s in range(2)]
        inner = [sb(f"inner{s}", [P, STEP_DUOS * PAIRS]) for s in range(RING)]
        hidden = [sb(f"hidden{s}", [P, STEP_DUOS * PAIRS]) for s in range(RING)]
        weight = sb("weight", [P, HALF])
        weighted = sb("weighted", [P, HALF])
        row_max = sb("row_max", [P, 1])
        exp_bias = sb("exp_bias", [P, 1])
        round_stats = sb("round_stats", [P, 3])
        stats = sb("stats", [P, ROUNDS * 3])
        first_half = sb("first_half", [P // 2, ROUNDS, 3])
        second_half = sb("second_half", [P // 2, ROUNDS, 3])
        top = sb("top", [P // 2, ROUNDS])
        down = [sb(f"down{n}", [P // 2, ROUNDS]) for n in range(2)]
        scale = [sb(f"scale{n}", [P // 2, ROUNDS]) for n in range(2)]
        part = [sb(f"part{n}", [P // 2, ROUNDS]) for n in range(4)]
        total = [sb(f"total{n}", [P // 2, ROUNDS]) for n in range(2)]
        inverse = sb("inverse", [P // 2, ROUNDS])
        ratio = sb("ratio", [P // 2, ROUNDS])
        y_rows = sb("y_rows", [P // 2, ROUNDS])
        y_out = sb("y_out", [ROUNDS, P // 2])

        h_bank = [pb(f"h_bank{n}", [P, 2 * BANK]) for n in range(2)]
        logit_bank = pb("logit_bank", [P, BANK])
        score_bank = pb("score_bank", [P, BANK])
        turn_bank = pb("turn_bank", [P, 2 * BANK])

        zeroed = sem("zeroed")
        ident_ready = sem("ident_ready")
        weights_loaded = sem("weights_loaded")
        w1_turned = sem("w1_turned")
        w1_ready = sem("w1_ready")
        x_loaded = [sem(f"x_loaded{s}") for s in range(2)]
        turned = sem("turned")
        xt_ready = sem("xt_ready")
        inner_ready = sem("inner_ready")
        h_ready = sem("h_ready")
        hidden_ready = sem("hidden_ready")
        steps_scored = sem("steps_scored")
        max_ready = sem("max_ready")
        dve_chain = sem("dve_chain")
        bias_ready = sem("bias_ready")
        exp_done = sem("exp_done")
        sums_done = sem("sums_done")
        stats_kept = sem("stats_kept")
        halves_moved = sem("halves_moved")
        down_ready = sem("down_ready")
        scale_ready = sem("scale_ready")
        y_ready = sem("y_ready")
        y_turned = sem("y_turned")
        y_copied = sem("y_copied")
        y_stored = sem("y_stored")

        x_chunks = x.rearrange("(h c b) f e -> h c (b f e)", h=2, b=CHUNK_DUOS).rearrange(
            "h c (p t e) -> h c p t e", p=P, t=TT)
        y_dram = y.rearrange("(a r k) o -> r a (k o)", a=2, k=ROUND_DUOS)

        block = ctx.enter_context(nc.Block())

        @block.sync
        def _(sp):
            sp.dma_start(b1_col[0:HIDDEN, :], b1.rearrange("(h o) -> h o", o=1)).then_inc(weights_loaded, 16)
            sp.dma_start(b1_col[HIDDEN:P, :], b1.rearrange("(h o) -> h o", o=1)).then_inc(weights_loaded, 16)
            sp.dma_start(b2_col[:, :], b2.rearrange("(h o) -> h o", o=1).to_broadcast([P, 1])).then_inc(weights_loaded, 16)
            sp.dma_start(bl_col[:, :], bl.rearrange("(h o) -> h o", o=1).to_broadcast([P, 1])).then_inc(weights_loaded, 16)

            def load_chunk(r, c):
                for half in range(2):
                    sp.dma_start(x_rows[c][:, :, half, :],
                                 x_chunks[half, r * CHUNKS_PER_ROUND + c]).then_inc(x_loaded[c], 16)

            for c in range(CHUNKS_PER_ROUND):
                load_chunk(0, c)
            sp.wait_ge(zeroed, 3)
            sp.dma_start(w1_rows[0:HIDDEN, 0:EMBED], w1).then_inc(weights_loaded, 16)
            sp.dma_start(w1_rows[HIDDEN:P, EMBED:P], w1).then_inc(weights_loaded, 16)
            for tile, row in ((w2_window, w2), (wl_window, wl)):
                for half in range(2):
                    sp.dma_start(tile[half * HIDDEN:(half + 1) * HIDDEN, MID + half:MID + half + 1],
                                 row.rearrange("o h -> h o")).then_inc(weights_loaded, 16)
            with sp.Fori(1, ROUNDS) as r:
                for c in range(CHUNKS_PER_ROUND):
                    sp.wait_ge(turned, (r - 1) * CHUNKS_PER_ROUND + c + 1)
                    load_chunk(r, c)

            sp.wait_ge(stats_kept, ROUNDS)
            for j in range(STEP_DUOS):
                for half, tile in enumerate((first_half, second_half)):
                    at = (2 * j + half) * QUAD
                    sp.dma_start(tile[j * QUAD:(j + 1) * QUAD, :, :],
                                 stats[at:at + QUAD, :].rearrange("p (r n) -> p r n", n=3)).then_inc(halves_moved, 16)
            sp.wait_ge(y_copied, 1)
            sp.dma_start(y_dram, y_out[:, :].rearrange("r (a k) -> r a k", a=2)).then_inc(y_stored, 16)
            sp.wait_ge(y_stored, 16)

        @block.gpsimd
        def _(pool):
            nc.gpsimd.memset(ident[:, :], 0.0).then_inc(ident_ready, 1)
            pool.wait_ge(ident_ready, 1)
            nc.gpsimd.affine_select(out=ident[:, :], in_=ident[:, :], compare_op=ALU.not_equal, fill=1.0,
                                    base=0, pattern=[[-1, P]], channel_multiplier=1).then_inc(ident_ready, 1)

        @block.tensor
        def _(pe):
            def turn_chunk(r, c):
                pe.wait_ge(x_loaded[c], 32 * (r + 1))
                if not (isinstance(r, int) and r == 0 and c == 0):
                    pe.wait_ge(xt_ready, 2 * (r * CHUNKS_PER_ROUND + c))
                for t in range(TT):
                    last = nc.tensor.transpose(turn_bank[:, t * P:(t + 1) * P],
                                               x_rows[c][:, t, :, :].rearrange("p h e -> p (h e)"), ident[:, :])
                last.then_inc(turned, 1)

            def hidden_layer(r, t):
                pe.wait_ge(inner_ready, 2 * (r * WINDOWS + t + 1))
                for j in range(STEP_DUOS):
                    if not (isinstance(r, int) and r == 0 and t == 0):
                        pe.wait_ge(hidden_ready, (r * WINDOWS + t) * STEP_DUOS + j - 1)
                    for half in range(2):
                        at = j * PAIRS + half * HALF
                        last = nc.tensor.matmul(h_bank[j][:, half * BANK:half * BANK + HALF], w1_block[:, :],
                                                inner[t % RING][:, at:at + HALF], start=True, stop=True)
                    last.then_inc(h_ready, 1)

            def score(r, t):
                pe.wait_ge(hidden_ready, (r * WINDOWS + t + 1) * STEP_DUOS)
                if t == 0 and not (isinstance(r, int) and r == 0):
                    pe.wait_ge(sums_done, r)
                window = slice(MID - 2 * t, MID - 2 * t + QUAD)
                for bank, weights, moving in ((logit_bank, w2_window, hidden), (score_bank, wl_window, inner)):
                    for g in range(2 * STEP_DUOS):
                        last = nc.tensor.matmul(bank[g * QUAD:(g + 1) * QUAD, 0:HALF], weights[:, window],
                                                moving[t % RING][:, g * HALF:(g + 1) * HALF],
                                                start=(t == 0), stop=(t == WINDOWS - 1),
                                                tile_position=(0, g * QUAD))
                last.then_inc(steps_scored, 1)

            def round_steps(r, first, last):
                for t in range(WINDOWS):
                    hidden_layer(r, t)
                    if t:
                        score(r, t - 1)
                    elif not first:
                        score(r - 1, WINDOWS - 1)
                    if t == CHUNK_STEPS // 2:
                        turn_chunk(r, 1)
                    if t == CHUNK_STEPS + CHUNK_STEPS // 2 and not last:
                        turn_chunk(r + 1, 0)

            pe.wait_ge(ident_ready, 2)
            pe.wait_ge(weights_loaded, 10 * 16)
            nc.tensor.transpose(h_bank[0][:, 0:P], w1_rows[:, :], ident[:, :]).then_inc(w1_turned, 1)
            turn_chunk(0, 0)
            pe.wait_ge(w1_ready, 1)
            round_steps(0, True, False)
            with pe.Fori(1, ROUNDS - 1) as r:
                round_steps(r, False, False)
            round_steps(ROUNDS - 1, False, True)
            score(ROUNDS - 1, WINDOWS - 1)

            pe.wait_ge(y_ready, 1)
            nc.tensor.transpose(turn_bank[0:ROUNDS, 0:P // 2], y_rows[:, :], ident[0:P // 2, 0:P // 2]).then_inc(
                y_turned, 1)

        @block.scalar
        def _(act):
            def copy_turned(r, c):
                act.wait_ge(turned, r * CHUNKS_PER_ROUND + c + 1)
                if not (isinstance(r, int) and r == 0):
                    act.wait_ge(inner_ready, 2 * ((r - 1) * WINDOWS + (c + 1) * CHUNK_STEPS))
                for fields, at in ((FIELDS, 0), (LAST, FIELDS)):
                    u = fields // TT
                    nc.scalar.copy(window_view(xt[c], at, [[EXT, CHUNK_DUOS], [TT, u], [1, TT]]),
                                   window_view(turn_bank, 0, [[U, CHUNK_DUOS], [1, u], [P, TT]])).then_inc(xt_ready, 1)

            def relu(r, t):
                if t >= RING or not (isinstance(r, int) and r == 0):
                    act.wait_ge(steps_scored, r * WINDOWS + t - RING + 1)
                for j in range(STEP_DUOS):
                    act.wait_ge(h_ready, (r * WINDOWS + t) * STEP_DUOS + j + 1)
                    nc.scalar.activation(
                        hidden[t % RING][:, j * PAIRS:(j + 1) * PAIRS].rearrange("p (a n) -> p a n", a=2),
                        h_bank[j][:, :].rearrange("p (a n) -> p a n", a=2)[:, :, 0:HALF],
                        ACT.Relu, bias=b1_col[:, 0:1]).then_inc(hidden_ready, 1)

            def exp_of_round(r):
                act.wait_ge(bias_ready, r + 1)
                if not (isinstance(r, int) and r == 0):
                    act.wait_ge(stats_kept, r)
                nc.scalar.activation(weight[:, :], logit_bank[:, 0:HALF], ACT.Exp, bias=exp_bias[:, 0:1],
                                     accum_out=round_stats[:, 1:2]).then_inc(exp_done, 1)

            def round_steps(r, first, last):
                for t in range(WINDOWS):
                    relu(r, t)
                    if t == 0 and not first:
                        exp_of_round(r - 1)
                    if t == CHUNK_STEPS // 2:
                        copy_turned(r, 1)
                    if t == CHUNK_STEPS + CHUNK_STEPS // 2 and not last:
                        copy_turned(r + 1, 0)

            act.wait_ge(w1_turned, 1)
            nc.scalar.copy(w1_block[:, :], h_bank[0][:, 0:P]).then_inc(w1_ready, 1)
            copy_turned(0, 0)
            round_steps(0, True, False)
            with act.Fori(1, ROUNDS - 1) as r:
                round_steps(r, False, False)
            round_steps(ROUNDS - 1, False, True)
            exp_of_round(ROUNDS - 1)

            for n in range(2):
                act.wait_ge(down_ready, n + 1)
                nc.scalar.activation(scale[n][:, :], down[n][:, :], ACT.Exp).then_inc(scale_ready, 1)
            act.wait_ge(y_turned, 1)
            nc.scalar.copy(y_out[:, :].rearrange("r (a k j) -> r a k j", a=2, j=STEP_DUOS),
                           turn_bank[0:ROUNDS, 0:P // 2].rearrange("r (j k a) -> r a k j", j=STEP_DUOS, a=2)
                           ).then_inc(y_copied, 1)

        @block.vector
        def _(dve):
            def products(r, t):
                c = t // CHUNK_STEPS
                if t % CHUNK_STEPS == 0:
                    dve.wait_ge(xt_ready, 2 * (r * CHUNKS_PER_ROUND + c + 1))
                if t >= RING or not (isinstance(r, int) and r == 0):
                    dve.wait_ge(steps_scored, r * WINDOWS + t - RING + 1)
                at = (t % CHUNK_STEPS) * STEP_DUOS * EXT
                nc.vector.tensor_tensor(
                    window_view(inner[t % RING], 0, [[PAIRS, STEP_DUOS], [FIELDS, SHIFTS], [1, FIELDS]]),
                    window_view(xt[c], at, [[EXT, STEP_DUOS], [0, SHIFTS], [1, FIELDS]]),
                    window_view(xt[c], at + 1, [[EXT, STEP_DUOS], [1, SHIFTS], [1, FIELDS]]),
                    ALU.mult).then_inc(inner_ready, 1)
                nc.vector.tensor_tensor(
                    window_view(inner[t % RING], SHIFTS * FIELDS, [[PAIRS, STEP_DUOS], [1, LAST]]),
                    window_view(xt[c], at, [[EXT, STEP_DUOS], [1, LAST]]),
                    window_view(xt[c], at + LAST, [[EXT, STEP_DUOS], [1, LAST]]),
                    ALU.mult).then_inc(inner_ready, 1)

            def softmax_of_round(r):
                dve.wait_ge(steps_scored, (r + 1) * WINDOWS)
                nc.vector.reduce_max(row_max[:, :], logit_bank[:, 0:HALF], AX_X).then_inc(max_ready, 1)
                dve.wait_ge(max_ready, r + 1)
                nc.vector.tensor_scalar(round_stats[:, 0:1], row_max[:, :], b2_col[:, 0:1], None,
                                        ALU.add).then_inc(dve_chain, 1)
                dve.wait_ge(dve_chain, r + 1)
                nc.vector.tensor_scalar(exp_bias[:, :], round_stats[:, 0:1], -1.0, b2_col[:, 0:1],
                                        ALU.mult, ALU.add).then_inc(bias_ready, 1)

            def sums_of_round(r):
                dve.wait_ge(exp_done, r + 1)
                nc.vector.tensor_tensor_reduce(out=weighted[:, :], in0=weight[:, :], in1=score_bank[:, 0:HALF],
                                               scale=1.0, scalar=0.0, op0=ALU.mult, op1=ALU.add,
                                               accum_out=round_stats[:, 2:3]).then_inc(sums_done, 1)
                dve.wait_ge(sums_done, r + 1)
                nc.vector.tensor_copy(stats[:, bass.ds(r * 3, 3)], round_stats[:, :]).then_inc(stats_kept, 1)

            def round_steps(r, first):
                for t in range(WINDOWS):
                    products(r, t)
                    if t == RING - 2 and not first:
                        softmax_of_round(r - 1)
                        sums_of_round(r - 1)

            dve.memset(w1_rows[:, :], 0.0).then_inc(zeroed, 1)
            dve.memset(w2_window[:, :], 0.0).then_inc(zeroed, 1)
            dve.memset(wl_window[:, :], 0.0).then_inc(zeroed, 1)
            dve.wait_ge(weights_loaded, 10 * 16)
            round_steps(0, True)
            with dve.Fori(1, ROUNDS) as r:
                round_steps(r, False)
            softmax_of_round(ROUNDS - 1)
            sums_of_round(ROUNDS - 1)

            dve.wait_ge(halves_moved, 4 * 16)
            chained = [ROUNDS]

            def chain(instruction):
                chained[0] += 1
                instruction.then_inc(dve_chain, 1)
                dve.wait_ge(dve_chain, chained[0])

            chain(nc.vector.tensor_tensor(top[:, :], first_half[:, :, 0], second_half[:, :, 0], ALU.max))
            nc.vector.tensor_tensor(down[0][:, :], first_half[:, :, 0], top[:, :], ALU.subtract).then_inc(down_ready, 1)
            nc.vector.tensor_tensor(down[1][:, :], second_half[:, :, 0], top[:, :], ALU.subtract).then_inc(down_ready, 1)
            dve.wait_ge(scale_ready, 2)
            for n in range(2):
                chain(nc.vector.tensor_tensor(part[2 * n][:, :], first_half[:, :, n + 1], scale[0][:, :], ALU.mult))
                chain(nc.vector.tensor_tensor(part[2 * n + 1][:, :], second_half[:, :, n + 1], scale[1][:, :], ALU.mult))
                chain(nc.vector.tensor_tensor(total[n][:, :], part[2 * n][:, :], part[2 * n + 1][:, :], ALU.add))
            chain(nc.vector.reciprocal(inverse[:, :], total[0][:, :]))
            chain(nc.vector.tensor_tensor(ratio[:, :], total[1][:, :], inverse[:, :], ALU.mult))
            nc.vector.tensor_scalar(y_rows[:, :], ratio[:, :], bl_col[0:P // 2, 0:1], None, ALU.add).then_inc(y_ready, 1)


_INS = ['r_x', 'L0_rec_W1', 'L0_rec_b1', 'L0_rec_W2', 'L0_rec_b2', 'L0_rec_Wl', 'L0_rec_bl']


def kernel(**inputs):
    import numpy as np
    import concourse.bacc as bacc
    from concourse.bass_utils import run_bass_kernel_spmd

    nc = bacc.Bacc("TRN2", target_bir_lowering=False, num_devices=1)
    arrays, args = {}, []
    for name in _INS:
        a = np.ascontiguousarray(inputs[name])
        arrays[f"in_{name}"] = a
        args.append(nc.dram_tensor(f"in_{name}", a.shape, mybir.dt.from_np(a.dtype), kind="ExternalInput").ap())
    y = nc.dram_tensor("out_y", (inputs['r_x'].shape[0], 1), F32, kind="ExternalOutput").ap()
    pair_attention_kernel(nc, *args, y)
    return run_bass_kernel_spmd(nc, [arrays], core_ids=[0]).results[0]["out_y"]
```

```python
from contextlib import ExitStack

import concourse.bass as bass
from concourse import mybir

F32 = mybir.dt.float32
F32R = mybir.dt.float32r
ALU = mybir.AluOpType
ACT = mybir.ActivationFunctionType
AX_X = mybir.AxisListType.X

P = 128


def window_view(tile, offset, dims, rows=slice(0, P)):
    whole = tile[rows, :]
    return bass.AP(whole.tensor, whole.offset + offset, [list(whole.ap[0])] + dims)


def pair_attention_kernel(nc, x, w1, b1, w2, b2, wl, bl, y):
    BATCH, FIELDS, EMBED = x.shape
    HIDDEN = w1.shape[0]
    assert EMBED == HIDDEN == P // 2

    DUOS = BATCH // 2
    SHIFTS = FIELDS // 2 - 1
    SPAN = FIELDS // 2
    LAST = SPAN // 2
    HALF = SHIFTS * SPAN + LAST
    PAIRS = 2 * HALF
    EXT = FIELDS + SPAN

    WINDOWS = 16
    STEP_DUOS = 2
    ROUND_DUOS = WINDOWS * STEP_DUOS
    ROUNDS = DUOS // ROUND_DUOS
    CHUNK_DUOS = 16
    CHUNK_STEPS = CHUNK_DUOS // STEP_DUOS
    CHUNKS_PER_ROUND = ROUND_DUOS // CHUNK_DUOS
    TT = CHUNK_DUOS * FIELDS // P
    U = FIELDS // TT
    RING = 4
    BANK = 512
    QUAD = 32
    SPLIT = [[True, t in (4, 6, 8, 10, 12, 14)] for t in range(WINDOWS)]
    SPLITS = sum(map(sum, SPLIT))
    LEAD = 2
    GRAM_ROWS = 2 * FIELDS
    GRAM_DUOS = CHUNK_DUOS // 2
    GRAM_STORES = 8
    assert P * TT == CHUNK_DUOS * FIELDS and U * TT == FIELDS and SPAN % TT == 0
    assert GRAM_DUOS * EXT <= BANK

    with ExitStack() as ctx:
        def sb(name, shape, dt=F32):
            return ctx.enter_context(nc.sbuf_tensor(name, shape, dt))

        def pb(name, shape):
            return ctx.enter_context(nc.psum_tensor(name, shape, F32))

        def sem(name):
            return ctx.enter_context(nc.semaphore(name))

        ident = sb("ident", [P, P])
        w1_rows = sb("w1_rows", [P, P])
        w1_block = sb("w1_block", [P, P])
        w1_high = sb("w1_high", [P, P], F32R)
        w1_low = sb("w1_low", [P, P], F32R)
        w2_window = sb("w2_window", [P, WINDOWS - 1 + QUAD])
        wl_col = sb("wl_col", [P, 1])
        b1_col = sb("b1_col", [P, 1])
        b2_col = sb("b2_col", [P, 1])
        bl_col = sb("bl_col", [P, 1])
        x_rows = [sb(f"x_rows{s}", [P, TT, 2, EMBED]) for s in range(2)]
        xt = [sb(f"xt{s}", [P, CHUNK_DUOS * EXT]) for s in range(2)]
        inner = [sb(f"inner{s}", [P, STEP_DUOS * PAIRS]) for s in range(RING)]
        inner_high = [sb(f"inner_high{s}", [P, STEP_DUOS * PAIRS], F32R) for s in range(RING)]
        inner_low = [sb(f"inner_low{s}", [P, STEP_DUOS * PAIRS], F32R) for s in range(RING)]
        x_scaled = sb("x_scaled", [P, CHUNK_DUOS * GRAM_ROWS])
        gram_rows = [sb(f"gram_rows{s}", [GRAM_ROWS, CHUNK_DUOS, EXT]) for s in range(2)]
        gram = sb("gram", [P, SPAN * FIELDS])
        hidden = [sb(f"hidden{s}", [P, STEP_DUOS * PAIRS]) for s in range(RING)]
        weight = sb("weight", [P, HALF])
        weighted = sb("weighted", [P, HALF])
        row_max = sb("row_max", [P, 1])
        exp_bias = sb("exp_bias", [P, 1])
        round_stats = sb("round_stats", [P, 4])
        stats = sb("stats", [P, ROUNDS, 4])
        second_half = sb("second_half", [P // 2, ROUNDS, 4])
        top = sb("top", [P // 2, ROUNDS])
        down = [sb(f"down{n}", [P // 2, ROUNDS]) for n in range(2)]
        scale = [sb(f"scale{n}", [P // 2, ROUNDS]) for n in range(2)]
        part = [sb(f"part{n}", [P // 2, ROUNDS]) for n in range(2)]
        total = [sb(f"total{n}", [P // 2, ROUNDS]) for n in range(3)]
        weighted_sum = sb("weighted_sum", [P // 2, ROUNDS])
        inverse = sb("inverse", [P // 2, ROUNDS])
        ratio = sb("ratio", [P // 2, ROUNDS])
        y_rows = sb("y_rows", [P // 2, ROUNDS])
        y_out = sb("y_out", [ROUNDS, P // 2])

        h_bank = [pb(f"h_bank{n}", [P, 2 * BANK]) for n in range(2)]
        logit_bank = pb("logit_bank", [P, BANK])
        gram_bank = pb("gram_bank", [GRAM_ROWS, BANK])
        turn_bank = pb("turn_bank", [P, 2 * BANK])

        zeroed = sem("zeroed")
        ident_ready = sem("ident_ready")
        weights_loaded = sem("weights_loaded")
        w1_turned = sem("w1_turned")
        w1_ready = sem("w1_ready")
        w1_high_ready = sem("w1_high_ready")
        w1_low_ready = sem("w1_low_ready")
        x_loaded = [sem(f"x_loaded{s}") for s in range(2)]
        turned = sem("turned")
        xt_ready = sem("xt_ready")
        scaled_ready = sem("scaled_ready")
        gram_ready = sem("gram_ready")
        gram_copied = sem("gram_copied")
        gram_stored = [sem(f"gram_stored{s}") for s in range(2)]
        gram_loaded = sem("gram_loaded")
        inner_ready = sem("inner_ready")
        high_ready = sem("high_ready")
        low_ready = sem("low_ready")
        h_ready = sem("h_ready")
        hidden_ready = sem("hidden_ready")
        steps_scored = sem("steps_scored")
        max_ready = sem("max_ready")
        dve_chain = sem("dve_chain")
        bias_ready = sem("bias_ready")
        exp_done = sem("exp_done")
        sums_done = sem("sums_done")
        stats_kept = sem("stats_kept")
        halves_moved = sem("halves_moved")
        down_ready = sem("down_ready")
        scale_ready = sem("scale_ready")
        y_ready = sem("y_ready")
        y_turned = sem("y_turned")
        y_copied = sem("y_copied")
        y_stored = sem("y_stored")

        gram_dram = nc.dram_tensor("gram_dram", (ROUNDS, 2, STEP_DUOS, 2, WINDOWS, SPAN, FIELDS), F32,
                                   kind="Internal").ap()
        def splits_to(r, t, j):
            return r * SPLITS + sum(map(sum, SPLIT[:t])) + sum(SPLIT[t][:j + 1])

        TURN_AT = [8, 0]
        GRAM_AT = [[12, 14], [4, 6]]
        GRAM_COPY_AT = [[13, 15], [5, 7]]
        EXP_AT = 1
        MAX_AT = RING

        x_chunks = x.rearrange("(h c b) f e -> h c (b f e)", h=2, b=CHUNK_DUOS).rearrange(
            "h c (p t e) -> h c p t e", p=P, t=TT)
        y_dram = y.rearrange("(a r k) o -> r a (k o)", a=2, k=ROUND_DUOS)

        block = ctx.enter_context(nc.Block())

        @block.sync
        def _(sp):
            sp.dma_start(b1_col[0:HIDDEN, :], b1.rearrange("(h o) -> h o", o=1)).then_inc(weights_loaded, 16)
            sp.dma_start(b1_col[HIDDEN:P, :], b1.rearrange("(h o) -> h o", o=1)).then_inc(weights_loaded, 16)
            sp.dma_start(b2_col[:, :], b2.rearrange("(h o) -> h o", o=1).to_broadcast([P, 1])).then_inc(weights_loaded, 16)
            sp.dma_start(bl_col[:, :], bl.rearrange("(h o) -> h o", o=1).to_broadcast([P, 1])).then_inc(weights_loaded, 16)

            def load_chunk(r, c):
                for half in range(2):
                    sp.dma_start(x_rows[c][:, :, half, :],
                                 x_chunks[half, r * CHUNKS_PER_ROUND + c]).then_inc(x_loaded[c], 16)

            def store_gram(r, c):
                sp.wait_ge(gram_copied, 2 * (r * CHUNKS_PER_ROUND + c + 1))
                for half in range(2):
                    for ab in range(2):
                        of = ab * FIELDS + half * SPAN
                        for j in range(STEP_DUOS):
                            sp.dma_start(
                                gram_dram[r, half, j, ab, c * CHUNK_STEPS:(c + 1) * CHUNK_STEPS].rearrange(
                                    "k i n -> i k n"),
                                gram_rows[c][of:of + SPAN, j::STEP_DUOS,
                                             half * SPAN:half * SPAN + FIELDS]).then_inc(gram_stored[c], 16)

            def load_gram(r):
                for c in range(CHUNKS_PER_ROUND):
                    sp.wait_ge(gram_stored[c], 16 * GRAM_STORES * (r + 1))
                if not (isinstance(r, int) and r == 0):
                    sp.wait_ge(stats_kept, r)
                sp.dma_start(gram[:, :], gram_dram[r].rearrange("h j a k i n -> (h j a k) (i n)")).then_inc(
                    gram_loaded, 16)

            def round_moves(r, last):
                for c in range(CHUNKS_PER_ROUND):
                    if not last:
                        sp.wait_ge(turned, r * CHUNKS_PER_ROUND + c + 1)
                        load_chunk(r + 1, c)
                    store_gram(r, c)
                load_gram(r)

            for c in range(CHUNKS_PER_ROUND):
                load_chunk(0, c)
            sp.wait_ge(zeroed, 2)
            sp.dma_start(w1_rows[0:HIDDEN, 0:EMBED], w1).then_inc(weights_loaded, 16)
            sp.dma_start(w1_rows[HIDDEN:P, EMBED:P], w1).then_inc(weights_loaded, 16)
            for half in range(2):
                at = (half + 1) * WINDOWS - 1
                sp.dma_start(w2_window[half * HIDDEN:(half + 1) * HIDDEN, at:at + 1],
                             w2.rearrange("o h -> h o")).then_inc(weights_loaded, 16)
                sp.dma_start(wl_col[half * EMBED:(half + 1) * EMBED, :],
                             wl.rearrange("o e -> e o")).then_inc(weights_loaded, 16)
            round_moves(0, False)
            with sp.Fori(1, ROUNDS - 1) as r:
                round_moves(r, False)
            round_moves(ROUNDS - 1, True)

            sp.wait_ge(stats_kept, ROUNDS)
            sp.dma_start(second_half[:, :, :], stats[P // 2:P, :, :]).then_inc(halves_moved, 16)
            sp.wait_ge(y_copied, 1)
            sp.dma_start(y_dram, y_out[:, :].rearrange("r (a k) -> r a k", a=2)).then_inc(y_stored, 16)
            sp.wait_ge(y_stored, 16)

        @block.gpsimd
        def _(pool):
            nc.gpsimd.memset(ident[:, :], 0.0).then_inc(ident_ready, 1)
            pool.wait_ge(ident_ready, 1)
            nc.gpsimd.affine_select(out=ident[:, :], in_=ident[:, :], compare_op=ALU.not_equal, fill=1.0,
                                    base=0, pattern=[[-1, P]], channel_multiplier=1).then_inc(ident_ready, 1)

        @block.tensor
        def _(pe):
            def turn_chunk(r, c):
                pe.wait_ge(x_loaded[c], 32 * (r + 1))
                if not (isinstance(r, int) and r == 0 and c == 0):
                    pe.wait_ge(xt_ready, 2 * (r * CHUNKS_PER_ROUND + c))
                for t in range(TT):
                    last = nc.tensor.transpose(turn_bank[:, t * P:(t + 1) * P],
                                               x_rows[c][:, t, :, :].rearrange("p h e -> p (h e)"), ident[:, :])
                last.then_inc(turned, 1)

            def gram_matrix(r, c, part):
                pe.wait_ge(scaled_ready, 2 * (r * CHUNKS_PER_ROUND + c + 1))
                if not (isinstance(r, int) and r == 0 and c == 0 and part == 0):
                    pe.wait_ge(gram_copied, 2 * (r * CHUNKS_PER_ROUND + c) + part)
                for n in range(GRAM_DUOS):
                    duo = part * GRAM_DUOS + n
                    last = nc.tensor.matmul(gram_bank[:, n * EXT:(n + 1) * EXT],
                                            x_scaled[:, duo * GRAM_ROWS:(duo + 1) * GRAM_ROWS],
                                            xt[c][:, duo * EXT:(duo + 1) * EXT], start=True, stop=True)
                last.then_inc(gram_ready, 1)

            def hidden_layer(r, t):
                slot = t % RING
                for j in range(STEP_DUOS):
                    if SPLIT[t][j]:
                        pe.wait_ge(low_ready, splits_to(r, t, j))
                    else:
                        pe.wait_ge(inner_ready, 3 * (r * WINDOWS + t + 1))
                    if not (isinstance(r, int) and r == 0 and t == 0):
                        pe.wait_ge(hidden_ready, (r * WINDOWS + t) * STEP_DUOS + j - 1)
                    if SPLIT[t][j]:
                        passes = ((w1_high, inner_low), (w1_low, inner_high), (w1_high, inner_high))
                    else:
                        passes = ((w1_block, inner),)
                    for half in range(2):
                        at = j * PAIRS + half * HALF
                        for n, (weights, moving) in enumerate(passes):
                            last = nc.tensor.matmul(h_bank[j][:, half * BANK:half * BANK + HALF], weights[:, :],
                                                    moving[slot][:, at:at + HALF],
                                                    start=(n == 0), stop=(n == len(passes) - 1))
                    last.then_inc(h_ready, 1)

            def score(r, t):
                pe.wait_ge(hidden_ready, (r * WINDOWS + t + 1) * STEP_DUOS)
                if t == 0 and not (isinstance(r, int) and r == 0):
                    pe.wait_ge(exp_done, r)
                first = WINDOWS - 1 - t
                for half in range(2):
                    for j in range(STEP_DUOS):
                        g = 2 * half + j
                        at = j * PAIRS + half * HALF
                        last = nc.tensor.matmul(logit_bank[g * QUAD:(g + 1) * QUAD, 0:HALF],
                                                w2_window[:, first:first + QUAD],
                                                hidden[t % RING][:, at:at + HALF],
                                                start=(t == 0), stop=(t == WINDOWS - 1),
                                                tile_position=(0, g * QUAD))
                last.then_inc(steps_scored, 1)

            def round_steps(r, first, last):
                for t in range(WINDOWS):
                    hidden_layer(r, t)
                    if t == 0 and not first:
                        score(r - 1, WINDOWS - 1)
                    if t == 2:
                        score(r, 0)
                    if t >= 2:
                        score(r, t - 1)
                    if t == TURN_AT[1]:
                        turn_chunk(r, 1)
                    if t == TURN_AT[0] and not last:
                        turn_chunk(r + 1, 0)
                    for part in range(2):
                        if t == GRAM_AT[1][part]:
                            gram_matrix(r, 1, part)
                        if t == GRAM_AT[0][part] and not last:
                            gram_matrix(r + 1, 0, part)

            pe.wait_ge(ident_ready, 2)
            pe.wait_ge(weights_loaded, 10 * 16)
            nc.tensor.transpose(h_bank[0][:, 0:P], w1_rows[:, :], ident[:, :]).then_inc(w1_turned, 1)
            turn_chunk(0, 0)
            pe.wait_ge(w1_ready, 1)
            pe.wait_ge(w1_high_ready, 1)
            pe.wait_ge(w1_low_ready, 1)
            gram_matrix(0, 0, 0)
            gram_matrix(0, 0, 1)
            round_steps(0, True, False)
            with pe.Fori(1, ROUNDS - 1) as r:
                round_steps(r, False, False)
            round_steps(ROUNDS - 1, False, True)
            score(ROUNDS - 1, WINDOWS - 1)

            pe.wait_ge(y_ready, 1)
            nc.tensor.transpose(turn_bank[0:ROUNDS, 0:P // 2], y_rows[:, :], ident[0:P // 2, 0:P // 2]).then_inc(
                y_turned, 1)

        @block.scalar
        def _(act):
            def copy_turned(r, c, part):
                chunk = r * CHUNKS_PER_ROUND + c
                if part == 0:
                    act.wait_ge(turned, chunk + 1)
                    if not (isinstance(r, int) and r == 0):
                        act.wait_ge(inner_ready, 3 * ((r - 1) * WINDOWS + (c + 1) * CHUNK_STEPS))
                    if not (isinstance(r, int) and r == 0 and c == 0):
                        act.wait_ge(gram_ready, 2 * chunk)
                    else:
                        act.wait_ge(zeroed, 3)
                if part < 2:
                    fields, at = ((FIELDS, 0), (SPAN, FIELDS))[part]
                    u = fields // TT
                    nc.scalar.copy(window_view(xt[c], at, [[EXT, CHUNK_DUOS], [TT, u], [1, TT]]),
                                   window_view(turn_bank, 0, [[U, CHUNK_DUOS], [1, u], [P, TT]])).then_inc(xt_ready, 1)
                else:
                    ab = part - 2
                    rows = slice(ab * EMBED, (ab + 1) * EMBED)
                    nc.scalar.activation(
                        window_view(x_scaled, ab * FIELDS, [[GRAM_ROWS, CHUNK_DUOS], [TT, U], [1, TT]], rows),
                        window_view(turn_bank, 0, [[U, CHUNK_DUOS], [1, U], [P, TT]], rows),
                        ACT.Copy, scale=wl_col[rows, 0:1]).then_inc(scaled_ready, 1)

            def copy_gram(r, c, part):
                act.wait_ge(gram_ready, 2 * (r * CHUNKS_PER_ROUND + c) + part + 1)
                if part == 0 and not (isinstance(r, int) and r == 0):
                    act.wait_ge(gram_stored[c], 16 * GRAM_STORES * r)
                nc.scalar.copy(gram_rows[c][:, part * GRAM_DUOS:(part + 1) * GRAM_DUOS, :],
                               gram_bank[:, 0:GRAM_DUOS * EXT].rearrange("p (d n) -> p d n", n=EXT)).then_inc(
                                   gram_copied, 1)

            def high_part(r, t, j):
                if not SPLIT[t][j]:
                    return
                if not (isinstance(r, int) and r == 0 and t < RING):
                    act.wait_ge(h_ready, (r * WINDOWS + t - RING + 1) * STEP_DUOS)
                act.wait_ge(inner_ready, 3 * (r * WINDOWS + t + 1))
                of = slice(j * PAIRS, (j + 1) * PAIRS)
                nc.scalar.copy(inner_high[t % RING][:, of], inner[t % RING][:, of]).then_inc(high_ready, 1)

            def relu(r, t, j):
                if j == 0 and not (isinstance(r, int) and r == 0 and t < RING):
                    act.wait_ge(steps_scored, r * WINDOWS + t - RING + 1)
                act.wait_ge(h_ready, (r * WINDOWS + t) * STEP_DUOS + j + 1)
                nc.scalar.activation(
                    hidden[t % RING][:, j * PAIRS:(j + 1) * PAIRS].rearrange("p (a n) -> p a n", a=2),
                    h_bank[j][:, :].rearrange("p (a n) -> p a n", a=2)[:, :, 0:HALF],
                    ACT.Relu, bias=b1_col[:, 0:1]).then_inc(hidden_ready, 1)

            def exp_of_round(r):
                act.wait_ge(bias_ready, r + 1)
                if not (isinstance(r, int) and r == 0):
                    act.wait_ge(stats_kept, r)
                nc.scalar.activation(weight[:, :], logit_bank[:, 0:HALF], ACT.Exp, bias=exp_bias[:, 0:1],
                                     accum_out=round_stats[:, 1:2]).then_inc(exp_done, 1)

            def round_steps(r, first, last):
                for t in range(WINDOWS):
                    for j in range(STEP_DUOS):
                        relu(r, t, j)
                        if t + LEAD < WINDOWS:
                            high_part(r, t + LEAD, j)
                        elif not last:
                            high_part(r + 1, t + LEAD - WINDOWS, j)
                    if t == EXP_AT and not first:
                        exp_of_round(r - 1)
                    if 0 <= t - TURN_AT[1] < 4:
                        copy_turned(r, 1, t - TURN_AT[1])
                    if 0 <= t - TURN_AT[0] < 4 and not last:
                        copy_turned(r + 1, 0, t - TURN_AT[0])
                    for part in range(2):
                        if t == GRAM_COPY_AT[1][part]:
                            copy_gram(r, 1, part)
                        if t == GRAM_COPY_AT[0][part] and not last:
                            copy_gram(r + 1, 0, part)

            act.wait_ge(w1_turned, 1)
            nc.scalar.copy(w1_block[:, :], h_bank[0][:, 0:P]).then_inc(w1_ready, 1)
            nc.scalar.copy(w1_high[:, :], h_bank[0][:, 0:P]).then_inc(w1_high_ready, 1)
            for n in range(4):
                copy_turned(0, 0, n)
            copy_gram(0, 0, 0)
            copy_gram(0, 0, 1)
            for t in range(LEAD):
                for j in range(STEP_DUOS):
                    high_part(0, t, j)
            round_steps(0, True, False)
            with act.Fori(1, ROUNDS - 1) as r:
                round_steps(r, False, False)
            round_steps(ROUNDS - 1, False, True)
            exp_of_round(ROUNDS - 1)

            for n in range(2):
                act.wait_ge(down_ready, n + 1)
                nc.scalar.activation(scale[n][:, :], down[n][:, :], ACT.Exp).then_inc(scale_ready, 1)
            act.wait_ge(y_turned, 1)
            nc.scalar.copy(y_out[:, :].rearrange("r (a k j) -> r a k j", a=2, j=STEP_DUOS),
                           turn_bank[0:ROUNDS, 0:P // 2].rearrange("r (j a k) -> r a k j", j=STEP_DUOS, a=2)
                           ).then_inc(y_copied, 1)

        @block.vector
        def _(dve):
            def products(r, t):
                c = t // CHUNK_STEPS
                if t % CHUNK_STEPS == 0:
                    dve.wait_ge(xt_ready, 2 * (r * CHUNKS_PER_ROUND + c + 1))
                if t >= RING or not (isinstance(r, int) and r == 0):
                    dve.wait_ge(h_ready, (r * WINDOWS + t - RING + 1) * STEP_DUOS)
                at = (t % CHUNK_STEPS) * STEP_DUOS * EXT
                for j in range(STEP_DUOS):
                    nc.vector.tensor_tensor(
                        window_view(inner[t % RING], j * PAIRS, [[HALF, 2], [SPAN, SHIFTS], [1, SPAN]]),
                        window_view(xt[c], at + j * EXT, [[SPAN, 2], [0, SHIFTS], [1, SPAN]]),
                        window_view(xt[c], at + j * EXT + 1, [[SPAN, 2], [1, SHIFTS], [1, SPAN]]),
                        ALU.mult).then_inc(inner_ready, 1)
                nc.vector.tensor_tensor(
                    window_view(inner[t % RING], SHIFTS * SPAN, [[PAIRS, STEP_DUOS], [HALF, 2], [1, LAST]]),
                    window_view(xt[c], at, [[EXT, STEP_DUOS], [SPAN + LAST, 2], [1, LAST]]),
                    window_view(xt[c], at + SPAN, [[EXT, STEP_DUOS], [SPAN + LAST, 2], [1, LAST]]),
                    ALU.mult).then_inc(inner_ready, 1)

            def low_parts(r, t):
                for j in range(STEP_DUOS):
                    if SPLIT[t][j]:
                        dve.wait_ge(high_ready, splits_to(r, t, j))
                        of = slice(j * PAIRS, (j + 1) * PAIRS)
                        nc.vector.tensor_tensor(inner_low[t % RING][:, of], inner[t % RING][:, of],
                                                inner_high[t % RING][:, of].bitcast(F32),
                                                ALU.subtract).then_inc(low_ready, 1)

            def softmax_of_round(r):
                dve.wait_ge(steps_scored, (r + 1) * WINDOWS)
                nc.vector.reduce_max(row_max[:, :], logit_bank[:, 0:HALF], AX_X).then_inc(max_ready, 1)
                dve.wait_ge(max_ready, r + 1)
                nc.vector.tensor_scalar(round_stats[:, 0:1], row_max[:, :], b2_col[:, 0:1], None,
                                        ALU.add).then_inc(dve_chain, 1)
                dve.wait_ge(dve_chain, r + 1)
                nc.vector.tensor_scalar(exp_bias[:, :], round_stats[:, 0:1], -1.0, b2_col[:, 0:1],
                                        ALU.mult, ALU.add).then_inc(bias_ready, 1)

            def sums_of_round(r):
                dve.wait_ge(exp_done, r + 1)
                dve.wait_ge(gram_loaded, 16 * (r + 1))
                main = SHIFTS * SPAN
                nc.vector.tensor_tensor_reduce(
                    out=weighted[:, 0:main].rearrange("p (d i) -> p d i", i=SPAN),
                    in0=weight[:, 0:main].rearrange("p (d i) -> p d i", i=SPAN),
                    in1=window_view(gram, 1, [[1, SHIFTS], [FIELDS + 1, SPAN]]),
                    scale=1.0, scalar=0.0, op0=ALU.mult, op1=ALU.add,
                    accum_out=round_stats[:, 2:3]).then_inc(sums_done, 1)
                for half in range(2):
                    rows = slice(half * P // 2, (half + 1) * P // 2)
                    nc.vector.tensor_tensor_reduce(
                        out=weighted[rows, main:HALF], in0=weight[rows, main:HALF],
                        in1=window_view(gram, SPAN + half * LAST * (FIELDS + 1), [[FIELDS + 1, LAST]], rows),
                        scale=1.0, scalar=0.0, op0=ALU.mult, op1=ALU.add,
                        accum_out=round_stats[rows, 3:4]).then_inc(sums_done, 1)
                dve.wait_ge(sums_done, 3 * (r + 1))
                nc.vector.tensor_copy(stats[:, bass.ds(r, 1), :],
                                      round_stats[:, :].rearrange("p (o n) -> p o n", o=1)).then_inc(stats_kept, 1)

            def round_steps(r, first):
                for t in range(WINDOWS):
                    products(r, t)
                    if t == MAX_AT and not first:
                        softmax_of_round(r - 1)
                    if t == MAX_AT + 1 and not first:
                        sums_of_round(r - 1)
                    if t:
                        low_parts(r, t - 1)
                    elif not first:
                        low_parts(r - 1, WINDOWS - 1)

            dve.memset(w1_rows[:, :], 0.0).then_inc(zeroed, 1)
            dve.memset(w2_window[:, :], 0.0).then_inc(zeroed, 1)
            dve.memset(x_scaled[:, :], 0.0).then_inc(zeroed, 1)
            dve.wait_ge(weights_loaded, 10 * 16)
            dve.wait_ge(w1_ready, 1)
            dve.wait_ge(w1_high_ready, 1)
            nc.vector.tensor_tensor(w1_low[:, :], w1_block[:, :], w1_high[:, :].bitcast(F32),
                                    ALU.subtract).then_inc(w1_low_ready, 1)
            round_steps(0, True)
            with dve.Fori(1, ROUNDS) as r:
                round_steps(r, False)
            low_parts(ROUNDS - 1, WINDOWS - 1)
            softmax_of_round(ROUNDS - 1)
            sums_of_round(ROUNDS - 1)

            dve.wait_ge(halves_moved, 16)
            first_half = stats[0:P // 2, :, :]
            chained = [ROUNDS]

            def chain(instruction):
                chained[0] += 1
                instruction.then_inc(dve_chain, 1)
                dve.wait_ge(dve_chain, chained[0])

            chain(nc.vector.tensor_tensor(top[:, :], first_half[:, :, 0], second_half[:, :, 0], ALU.max))
            nc.vector.tensor_tensor(down[0][:, :], first_half[:, :, 0], top[:, :], ALU.subtract).then_inc(down_ready, 1)
            nc.vector.tensor_tensor(down[1][:, :], second_half[:, :, 0], top[:, :], ALU.subtract).then_inc(down_ready, 1)
            dve.wait_ge(scale_ready, 2)
            for n, column in ((0, 1), (1, 2), (2, 3)):
                chain(nc.vector.tensor_tensor(part[0][:, :], first_half[:, :, column], scale[0][:, :], ALU.mult))
                chain(nc.vector.tensor_tensor(part[1][:, :], second_half[:, :, column], scale[1][:, :], ALU.mult))
                chain(nc.vector.tensor_tensor(total[n][:, :], part[0][:, :], part[1][:, :], ALU.add))
            chain(nc.vector.tensor_tensor(weighted_sum[:, :], total[1][:, :], total[2][:, :], ALU.add))
            chain(nc.vector.reciprocal(inverse[:, :], total[0][:, :]))
            chain(nc.vector.tensor_tensor(ratio[:, :], weighted_sum[:, :], inverse[:, :], ALU.mult))
            nc.vector.tensor_scalar(y_rows[:, :], ratio[:, :], bl_col[0:P // 2, 0:1], None, ALU.add).then_inc(y_ready, 1)


_INS = ['r_x', 'L0_rec_W1', 'L0_rec_b1', 'L0_rec_W2', 'L0_rec_b2', 'L0_rec_Wl', 'L0_rec_bl']


def kernel(**inputs):
    import numpy as np
    import concourse.bacc as bacc
    from concourse.bass_utils import run_bass_kernel_spmd

    nc = bacc.Bacc("TRN2", target_bir_lowering=False, num_devices=1)
    arrays, args = {}, []
    for name in _INS:
        a = np.ascontiguousarray(inputs[name])
        arrays[f"in_{name}"] = a
        args.append(nc.dram_tensor(f"in_{name}", a.shape, mybir.dt.from_np(a.dtype), kind="ExternalInput").ap())
    y = nc.dram_tensor("out_y", (inputs['r_x'].shape[0], 1), F32, kind="ExternalOutput").ap()
    pair_attention_kernel(nc, *args, y)
    return run_bass_kernel_spmd(nc, [arrays], core_ids=[0]).results[0]["out_y"]
```

```python
from contextlib import ExitStack

import concourse.bass as bass
from concourse import mybir

F32 = mybir.dt.float32
F32R = mybir.dt.float32r
ALU = mybir.AluOpType
ACT = mybir.ActivationFunctionType
AX_X = mybir.AxisListType.X

P = 128


def window_view(tile, offset, dims, rows=slice(0, P)):
    whole = tile[rows, :]
    return bass.AP(whole.tensor, whole.offset + offset, [list(whole.ap[0])] + dims)


def pair_attention_kernel(nc, x, w1, b1, w2, b2, wl, bl, y):
    BATCH, FIELDS, EMBED = x.shape
    HIDDEN = w1.shape[0]
    assert EMBED == HIDDEN == P // 2

    DUOS = BATCH // 2
    SHIFTS = FIELDS // 2 - 1
    SPAN = FIELDS // 2
    LAST = SPAN // 2
    HALF = SHIFTS * SPAN + LAST
    PAIRS = 2 * HALF
    EXT = FIELDS + SPAN

    WINDOWS = 16
    STEP_DUOS = 2
    ROUND_DUOS = WINDOWS * STEP_DUOS
    ROUNDS = DUOS // ROUND_DUOS
    CHUNK_DUOS = 16
    CHUNK_STEPS = CHUNK_DUOS // STEP_DUOS
    CHUNKS_PER_ROUND = ROUND_DUOS // CHUNK_DUOS
    TT = CHUNK_DUOS * FIELDS // P
    U = FIELDS // TT
    RING = 4
    INNER_RING = 8
    STEP = STEP_DUOS * PAIRS
    BANK = 512
    QUAD = 32
    BOTH_SPLIT = (1, 2, 5, 7, 9, 11, 13, 15)
    SPLIT = [2 if t in BOTH_SPLIT else 1 for t in range(WINDOWS)]
    LEAD = 3
    LOW_LAG = 2
    TILE = P // 2
    GRAM_COLUMNS = 2 * SPAN
    GRAM_DUOS = CHUNK_DUOS // 2
    GRAM_AT_COLUMN = TT * P
    GRAM_END = GRAM_AT_COLUMN + GRAM_DUOS * FIELDS
    GRAM_STORES = 8
    assert P * TT == CHUNK_DUOS * FIELDS and U * TT == FIELDS and SPAN % TT == 0
    assert BANK <= GRAM_AT_COLUMN and GRAM_END <= 2 * BANK and GRAM_COLUMNS <= TILE

    with ExitStack() as ctx:
        def sb(name, shape, dt=F32):
            return ctx.enter_context(nc.sbuf_tensor(name, shape, dt))

        def pb(name, shape):
            return ctx.enter_context(nc.psum_tensor(name, shape, F32))

        def sem(name):
            return ctx.enter_context(nc.semaphore(name))

        ident = sb("ident", [P, P])
        w1_rows = sb("w1_rows", [P, P])
        w1_block = sb("w1_block", [P, P])
        w1_high = sb("w1_high", [P, P], F32R)
        w1_low = sb("w1_low", [P, P], F32R)
        w2_window = sb("w2_window", [P, WINDOWS - 1 + QUAD])
        wl_col = sb("wl_col", [P, 1])
        b1_col = sb("b1_col", [P, 1])
        b2_col = sb("b2_col", [P, 1])
        bl_col = sb("bl_col", [P, 1])
        x_rows = [sb(f"x_rows{s}", [P, TT, 2, EMBED]) for s in range(2)]
        xt = [sb(f"xt{s}", [P, CHUNK_DUOS * EXT]) for s in range(2)]
        inner = sb("inner", [P, INNER_RING * STEP])
        inner_high = [sb(f"inner_high{s}", [P, STEP], F32R) for s in range(RING)]
        inner_low = [sb(f"inner_low{s}", [P, STEP], F32R) for s in range(RING)]
        x_scaled = sb("x_scaled", [P, CHUNK_DUOS * 2 * GRAM_COLUMNS])
        gram_rows = [sb(f"gram_rows{s}", [P, CHUNK_DUOS, FIELDS]) for s in range(2)]
        gram = sb("gram", [P, SPAN * FIELDS])
        hidden = [sb(f"hidden{s}", [P, STEP]) for s in range(RING)]
        weight = sb("weight", [P, HALF])
        weighted = sb("weighted", [P, HALF])
        row_max = sb("row_max", [P, 1])
        exp_bias = sb("exp_bias", [P, 1])
        round_stats = sb("round_stats", [P, 4])
        stats = sb("stats", [P, 4, ROUNDS])
        maxima = sb("maxima", [ROUNDS, 2, P // 2])
        top = sb("top", [ROUNDS, P // 2])
        down = sb("down", [ROUNDS, 2, P // 2])
        scale = sb("scale", [ROUNDS, P])
        part = sb("part", [ROUNDS, 3, P])
        total = sb("total", [ROUNDS, 3, P // 2])
        weighted_sum = sb("weighted_sum", [ROUNDS, P // 2])
        inverse = sb("inverse", [ROUNDS, P // 2])
        ratio = sb("ratio", [ROUNDS, P // 2])
        y_out = sb("y_out", [ROUNDS, P // 2])

        h_bank = [pb(f"h_bank{n}", [P, 2 * BANK]) for n in range(2)]
        logit_bank = [pb(f"logit_bank{n}", [P, BANK]) for n in range(2)]
        turn_bank = pb("turn_bank", [P, 2 * BANK])

        zeroed = sem("zeroed")
        ident_ready = sem("ident_ready")
        w1_loaded = sem("w1_loaded")
        wl_loaded = sem("wl_loaded")
        b1_loaded = sem("b1_loaded")
        w2_loaded = sem("w2_loaded")
        offsets_loaded = sem("offsets_loaded")
        w1_turned = sem("w1_turned")
        w1_ready = sem("w1_ready")
        w1_high_ready = sem("w1_high_ready")
        w1_low_ready = sem("w1_low_ready")
        x_loaded = [sem(f"x_loaded{s}") for s in range(2)]
        turned = sem("turned")
        xt_ready = sem("xt_ready")
        scaled_ready = sem("scaled_ready")
        gram_ready = sem("gram_ready")
        gram_copied = sem("gram_copied")
        gram_stored = [sem(f"gram_stored{s}") for s in range(2)]
        gram_loaded = sem("gram_loaded")
        inner_ready = sem("inner_ready")
        high_ready = sem("high_ready")
        low_ready = sem("low_ready")
        h_ready = sem("h_ready")
        hidden_ready = sem("hidden_ready")
        steps_scored = sem("steps_scored")
        max_ready = sem("max_ready")
        dve_chain = sem("dve_chain")
        bias_ready = sem("bias_ready")
        exp_done = sem("exp_done")
        sums_done = sem("sums_done")
        stats_kept = sem("stats_kept")
        stats_turned = sem("stats_turned")
        down_ready = sem("down_ready")
        scale_ready = sem("scale_ready")
        y_ready = sem("y_ready")
        y_stored = sem("y_stored")

        gram_dram = nc.dram_tensor("gram_dram", (ROUNDS, 2, STEP_DUOS, 2, WINDOWS, SPAN, FIELDS), F32,
                                   kind="Internal").ap()

        def inner_to(r, t):
            return 5 * (r * (WINDOWS // 2) + t // 2 + 1)

        def split_products(t):
            at = (t % INNER_RING) * STEP
            return inner[:, at:at + SPLIT[t] * PAIRS]

        TURN_AT = [8, 0]
        TURN_COPY_AT = [[8, 9, 11, 11], [0, 0, 2, 3]]
        GRAM_AT = [[12, 14], [4, 6]]
        GRAM_COPY_AT = [[13, 15], [5, 6]]
        EXP_AT = 3
        MAX_AT = 7
        SUMS_AT = 8

        x_chunks = x.rearrange("(h c b) f e -> h c (b f e)", h=2, b=CHUNK_DUOS).rearrange(
            "h c (p t e) -> h c p t e", p=P, t=TT)
        y_dram = y.rearrange("(a r k) o -> r a (k o)", a=2, k=ROUND_DUOS)

        block = ctx.enter_context(nc.Block())

        @block.sync
        def _(sp):
            def load_chunk(r, c):
                for half in range(2):
                    sp.dma_start(x_rows[c][:, :, half, :],
                                 x_chunks[half, r * CHUNKS_PER_ROUND + c]).then_inc(x_loaded[c], 16)

            def store_gram(r, c):
                sp.wait_ge(gram_copied, 2 * (r * CHUNKS_PER_ROUND + c + 1))
                for half in range(2):
                    for ab in range(2):
                        of = half * TILE + ab * SPAN
                        for j in range(STEP_DUOS):
                            sp.dma_start(
                                gram_dram[r, half, j, ab, c * CHUNK_STEPS:(c + 1) * CHUNK_STEPS].rearrange(
                                    "k i n -> i k n"),
                                gram_rows[c][of:of + SPAN, j::STEP_DUOS, :]).then_inc(gram_stored[c], 16)

            def load_gram(r):
                for c in range(CHUNKS_PER_ROUND):
                    sp.wait_ge(gram_stored[c], 16 * GRAM_STORES * (r + 1))
                if not (isinstance(r, int) and r == 0):
                    sp.wait_ge(stats_kept, r)
                sp.dma_start(gram[:, :], gram_dram[r].rearrange("h j a k i n -> (h j a k) (i n)")).then_inc(
                    gram_loaded, 16)

            def round_moves(r, last):
                for c in range(CHUNKS_PER_ROUND):
                    if not last:
                        sp.wait_ge(turned, r * CHUNKS_PER_ROUND + c + 1)
                        load_chunk(r + 1, c)
                    store_gram(r, c)
                load_gram(r)

            halves = [slice(half * HIDDEN, (half + 1) * HIDDEN) for half in range(2)]
            load_chunk(0, 0)
            sp.wait_ge(zeroed, 1)
            for rows in halves:
                sp.dma_start(w1_rows[rows, rows], w1).then_inc(w1_loaded, 16)
            for rows in halves:
                sp.dma_start(wl_col[rows, :], wl.rearrange("o e -> e o")).then_inc(wl_loaded, 16)
            for rows in halves:
                sp.dma_start(b1_col[rows, :], b1.rearrange("(h o) -> h o", o=1)).then_inc(b1_loaded, 16)
            sp.wait_ge(zeroed, 2)
            for half, rows in enumerate(halves):
                at = (half + 1) * WINDOWS - 1
                sp.dma_start(w2_window[rows, at:at + 1], w2.rearrange("o h -> h o")).then_inc(w2_loaded, 16)
            load_chunk(0, 1)
            for column, value in ((b2_col, b2), (bl_col, bl)):
                sp.dma_start(column[:, :], value.rearrange("(h o) -> h o", o=1).to_broadcast([P, 1])).then_inc(
                    offsets_loaded, 16)
            round_moves(0, False)
            with sp.Fori(1, ROUNDS - 1) as r:
                round_moves(r, False)
            round_moves(ROUNDS - 1, True)

            sp.wait_ge(y_ready, 1)
            sp.dma_start(y_dram, y_out[:, :].rearrange("r (a k) -> r a k", a=2)).then_inc(y_stored, 16)
            sp.wait_ge(y_stored, 16)

        @block.gpsimd
        def _(pool):
            nc.gpsimd.memset(ident[:, :], 0.0).then_inc(ident_ready, 1)
            pool.wait_ge(ident_ready, 1)
            nc.gpsimd.affine_select(out=ident[:, :], in_=ident[:, :], compare_op=ALU.not_equal, fill=1.0,
                                    base=0, pattern=[[-1, P]], channel_multiplier=1).then_inc(ident_ready, 1)

        @block.tensor
        def _(pe):
            def turn_chunk(r, c):
                pe.wait_ge(x_loaded[c], 32 * (r + 1))
                if not (isinstance(r, int) and r == 0 and c == 0):
                    pe.wait_ge(gram_copied, 2 * (r * CHUNKS_PER_ROUND + c))
                for t in range(TT):
                    last = nc.tensor.transpose(turn_bank[:, t * P:(t + 1) * P],
                                               x_rows[c][:, t, :, :].rearrange("p h e -> p (h e)"), ident[:, :])
                last.then_inc(turned, 1)

            def gram_matrix(r, c, part):
                pe.wait_ge(scaled_ready, 2 * (r * CHUNKS_PER_ROUND + c + 1))
                if not (isinstance(r, int) and r == 0 and c == 0 and part == 0):
                    pe.wait_ge(gram_copied, 2 * (r * CHUNKS_PER_ROUND + c) + part)
                for n in range(GRAM_DUOS):
                    duo = part * GRAM_DUOS + n
                    for half in range(2):
                        scaled_at = (2 * duo + half) * GRAM_COLUMNS
                        fields_at = duo * EXT + half * SPAN
                        last = nc.tensor.matmul(
                            turn_bank[half * TILE:half * TILE + GRAM_COLUMNS,
                                      GRAM_AT_COLUMN + n * FIELDS:GRAM_AT_COLUMN + (n + 1) * FIELDS],
                            x_scaled[:, scaled_at:scaled_at + GRAM_COLUMNS],
                            xt[c][:, fields_at:fields_at + FIELDS], start=True, stop=True,
                            tile_position=(0, half * TILE))
                last.then_inc(gram_ready, 1)

            def hidden_layer(r, t):
                slot = t % RING
                split = 0 if isinstance(r, int) and r == 0 and t < LEAD else SPLIT[t]
                if isinstance(r, int) and r == 0 and t == LEAD:
                    pe.wait_ge(w1_low_ready, 1)
                for j in range(STEP_DUOS):
                    if j < split:
                        pe.wait_ge(low_ready, r * WINDOWS + t + 1 - LEAD)
                    else:
                        pe.wait_ge(inner_ready, inner_to(r, t))
                    if not (isinstance(r, int) and r == 0 and t == 0):
                        pe.wait_ge(hidden_ready, (r * WINDOWS + t) * STEP_DUOS + j - 1)
                    if j < split:
                        passes = ((w1_high, inner_low[slot], 0), (w1_low, inner_high[slot], 0),
                                  (w1_high, inner_high[slot], 0))
                    else:
                        passes = ((w1_block, inner, (t % INNER_RING) * STEP),)
                    for half in range(2):
                        for n, (weights, moving, base) in enumerate(passes):
                            at = base + j * PAIRS + half * HALF
                            last = nc.tensor.matmul(h_bank[j][:, half * BANK:half * BANK + HALF], weights[:, :],
                                                    moving[:, at:at + HALF],
                                                    start=(n == 0), stop=(n == len(passes) - 1))
                    last.then_inc(h_ready, 1)

            def score(r, t, bank):
                pe.wait_ge(hidden_ready, (r * WINDOWS + t + 1) * STEP_DUOS)
                if t == 0 and isinstance(r, int) and r == 0:
                    pe.wait_ge(w2_loaded, 2 * 16)
                first = WINDOWS - 1 - t
                for half in range(2):
                    for j in range(STEP_DUOS):
                        g = 2 * half + j
                        at = j * PAIRS + half * HALF
                        last = nc.tensor.matmul(bank[g * QUAD:(g + 1) * QUAD, 0:HALF],
                                                w2_window[:, first:first + QUAD],
                                                hidden[t % RING][:, at:at + HALF],
                                                start=(t == 0), stop=(t == WINDOWS - 1),
                                                tile_position=(0, g * QUAD))
                last.then_inc(steps_scored, 1)

            def round_steps(r, odd, first=False, last=False):
                for t in range(WINDOWS):
                    hidden_layer(r, t)
                    if t:
                        score(r, t - 1, logit_bank[odd])
                    elif not first:
                        score(r - 1, WINDOWS - 1, logit_bank[1 - odd])
                    if first and t == 0:
                        gram_matrix(r, 0, 1)
                    for part in range(2):
                        if t == GRAM_AT[1][part] + first:
                            gram_matrix(r, 1, part)
                        if t == GRAM_AT[0][part] and not last:
                            gram_matrix(r + 1, 0, part)
                    if t == TURN_AT[1] + first:
                        turn_chunk(r, 1)
                    if t == TURN_AT[0] and not last:
                        turn_chunk(r + 1, 0)

            pe.wait_ge(ident_ready, 2)
            pe.wait_ge(zeroed, 4)
            turn_chunk(0, 0)
            pe.wait_ge(w1_loaded, 2 * 16)
            nc.tensor.transpose(h_bank[0][:, 0:P], w1_rows[:, :], ident[:, :]).then_inc(w1_turned, 1)
            pe.wait_ge(w1_ready, 1)
            pe.wait_ge(w1_high_ready, 1)
            gram_matrix(0, 0, 0)
            round_steps(0, 0, first=True)
            with pe.Fori(0, ROUNDS // 2 - 1) as pair:
                round_steps(2 * pair + 1, 1)
                round_steps(2 * pair + 2, 0)
            round_steps(ROUNDS - 1, 1, last=True)
            score(ROUNDS - 1, WINDOWS - 1, logit_bank[1])

            pe.wait_ge(stats_kept, ROUNDS)
            for n in range(4):
                last = nc.tensor.transpose(turn_bank[0:ROUNDS, n * P:(n + 1) * P], stats[:, n, :], ident[:, :])
            last.then_inc(stats_turned, 1)

        @block.scalar
        def _(act):
            def copy_turned(r, c, part):
                chunk = r * CHUNKS_PER_ROUND + c
                if part == 0:
                    act.wait_ge(turned, chunk + 1)
                    if not (isinstance(r, int) and r == 0):
                        act.wait_ge(inner_ready, inner_to(r - 1, (c + 1) * CHUNK_STEPS - 1))
                        act.wait_ge(gram_ready, 2 * (chunk - 1))
                if part < 2:
                    fields, at = ((FIELDS, 0), (SPAN, FIELDS))[part]
                    u = fields // TT
                    nc.scalar.copy(window_view(xt[c], at, [[EXT, CHUNK_DUOS], [TT, u], [1, TT]]),
                                   window_view(turn_bank, 0, [[U, CHUNK_DUOS], [1, u], [P, TT]])).then_inc(xt_ready, 1)
                else:
                    if isinstance(r, int) and r == 0 and c == 0:
                        act.wait_ge(zeroed, 3)
                        act.wait_ge(wl_loaded, 2 * 16)
                    elif part == 2:
                        act.wait_ge(gram_ready, 2 * chunk)
                    ab = part - 2
                    rows = slice(ab * EMBED, (ab + 1) * EMBED)
                    nc.scalar.activation(
                        window_view(x_scaled, ab * SPAN, [[GRAM_COLUMNS, 2 * CHUNK_DUOS], [TT, U // 2], [1, TT]],
                                    rows),
                        window_view(turn_bank, 0, [[U // 2, 2 * CHUNK_DUOS], [1, U // 2], [P, TT]], rows),
                        ACT.Copy, scale=wl_col[rows, 0:1]).then_inc(scaled_ready, 1)

            def copy_gram(r, c, part):
                act.wait_ge(gram_ready, 2 * (r * CHUNKS_PER_ROUND + c) + part + 1)
                if part == 0 and not (isinstance(r, int) and r == 0):
                    act.wait_ge(gram_stored[c], 16 * GRAM_STORES * r)
                nc.scalar.copy(gram_rows[c][:, part * GRAM_DUOS:(part + 1) * GRAM_DUOS, :],
                               turn_bank[:, GRAM_AT_COLUMN:GRAM_END].rearrange("p (d n) -> p d n", n=FIELDS)).then_inc(
                                   gram_copied, 1)

            def high_part(r, t):
                if not (isinstance(r, int) and r == 0 and t < RING):
                    act.wait_ge(h_ready, (r * WINDOWS + t - RING + 1) * STEP_DUOS)
                act.wait_ge(inner_ready, inner_to(r, t))
                of = slice(0, SPLIT[t] * PAIRS)
                nc.scalar.copy(inner_high[t % RING][:, of], split_products(t)).then_inc(high_ready, 1)

            def relu(r, t, j):
                if j == 0 and not (isinstance(r, int) and r == 0 and t < RING):
                    act.wait_ge(steps_scored, r * WINDOWS + t - RING + 1)
                act.wait_ge(h_ready, (r * WINDOWS + t) * STEP_DUOS + j + 1)
                nc.scalar.activation(
                    hidden[t % RING][:, j * PAIRS:(j + 1) * PAIRS].rearrange("p (a n) -> p a n", a=2),
                    h_bank[j][:, :].rearrange("p (a n) -> p a n", a=2)[:, :, 0:HALF],
                    ACT.Relu, bias=b1_col[:, 0:1]).then_inc(hidden_ready, 1)

            def exp_of_round(r, bank):
                act.wait_ge(bias_ready, r + 1)
                nc.scalar.activation(weight[:, :], bank[:, 0:HALF], ACT.Exp, bias=exp_bias[:, 0:1],
                                     accum_out=round_stats[:, 1:2]).then_inc(exp_done, 1)

            def round_steps(r, odd, first=False, last=False):
                for t in range(WINDOWS):
                    for j in range(STEP_DUOS):
                        relu(r, t, j)
                    if t + LEAD < WINDOWS:
                        high_part(r, t + LEAD)
                    elif not last:
                        high_part(r + 1, t + LEAD - WINDOWS)
                    if t == EXP_AT and not first:
                        exp_of_round(r - 1, logit_bank[1 - odd])
                    if first and t == 0:
                        copy_gram(r, 0, 1)
                    for part in range(2):
                        if t == GRAM_COPY_AT[1][part] + first:
                            copy_gram(r, 1, part)
                        if t == GRAM_COPY_AT[0][part] and not last:
                            copy_gram(r + 1, 0, part)
                    for part in range(4):
                        if t == TURN_COPY_AT[1][part] + first:
                            copy_turned(r, 1, part)
                        if t == TURN_COPY_AT[0][part] and not last:
                            copy_turned(r + 1, 0, part)

            for n in range(2):
                copy_turned(0, 0, n)
            act.wait_ge(w1_turned, 1)
            nc.scalar.copy(w1_block[:, :], h_bank[0][:, 0:P]).then_inc(w1_ready, 1)
            nc.scalar.copy(w1_high[:, :], h_bank[0][:, 0:P]).then_inc(w1_high_ready, 1)
            for n in range(2, 4):
                copy_turned(0, 0, n)
            copy_gram(0, 0, 0)
            act.wait_ge(b1_loaded, 2 * 16)
            round_steps(0, 0, first=True)
            with act.Fori(0, ROUNDS // 2 - 1) as pair:
                round_steps(2 * pair + 1, 1)
                round_steps(2 * pair + 2, 0)
            round_steps(ROUNDS - 1, 1, last=True)
            exp_of_round(ROUNDS - 1, logit_bank[1])

            act.wait_ge(down_ready, 1)
            nc.scalar.activation(scale[:, :], down[:, :, :].rearrange("r h s -> r (h s)"), ACT.Exp).then_inc(
                scale_ready, 1)

        @block.vector
        def _(dve):
            def products(r, t):
                c = t // CHUNK_STEPS
                if t % CHUNK_STEPS == 0:
                    dve.wait_ge(xt_ready, 2 * (r * CHUNKS_PER_ROUND + c + 1))
                if t >= INNER_RING or not (isinstance(r, int) and r == 0):
                    dve.wait_ge(h_ready, (r * WINDOWS + t - INNER_RING + 1) * STEP_DUOS)
                to = (t % INNER_RING) * STEP
                at = (t % CHUNK_STEPS) * STEP_DUOS * EXT
                for j in range(STEP_DUOS):
                    nc.vector.tensor_tensor(
                        window_view(inner, to + j * PAIRS, [[HALF, 2], [SPAN, SHIFTS], [1, SPAN]]),
                        window_view(xt[c], at + j * EXT, [[SPAN, 2], [0, SHIFTS], [1, SPAN]]),
                        window_view(xt[c], at + j * EXT + 1, [[SPAN, 2], [1, SHIFTS], [1, SPAN]]),
                        ALU.mult).then_inc(inner_ready, 1)
                if t % 2:
                    to, at, duos = to - STEP, at - STEP_DUOS * EXT, 2 * STEP_DUOS
                    nc.vector.tensor_tensor(
                        window_view(inner, to + SHIFTS * SPAN, [[PAIRS, duos], [HALF, 2], [1, LAST]]),
                        window_view(xt[c], at, [[EXT, duos], [SPAN + LAST, 2], [1, LAST]]),
                        window_view(xt[c], at + SPAN, [[EXT, duos], [SPAN + LAST, 2], [1, LAST]]),
                        ALU.mult).then_inc(inner_ready, 1)

            def low_parts(r, t):
                dve.wait_ge(high_ready, r * WINDOWS + t + 1 - LEAD)
                if not (isinstance(r, int) and r == 0 and t < RING):
                    dve.wait_ge(h_ready, (r * WINDOWS + t - RING + 1) * STEP_DUOS)
                of = slice(0, SPLIT[t] * PAIRS)
                nc.vector.tensor_tensor(inner_low[t % RING][:, of], split_products(t),
                                        inner_high[t % RING][:, of].bitcast(F32),
                                        ALU.subtract).then_inc(low_ready, 1)

            def softmax_of_round(r, bank):
                dve.wait_ge(steps_scored, (r + 1) * WINDOWS)
                nc.vector.reduce_max(row_max[:, :], bank[:, 0:HALF], AX_X).then_inc(max_ready, 1)
                dve.wait_ge(max_ready, r + 1)
                nc.vector.tensor_scalar(round_stats[:, 0:1], row_max[:, :], b2_col[:, 0:1], None,
                                        ALU.add).then_inc(dve_chain, 1)
                dve.wait_ge(dve_chain, r + 1)
                nc.vector.tensor_scalar(exp_bias[:, :], round_stats[:, 0:1], -1.0, b2_col[:, 0:1],
                                        ALU.mult, ALU.add).then_inc(bias_ready, 1)

            def sums_of_round(r):
                dve.wait_ge(exp_done, r + 1)
                dve.wait_ge(gram_loaded, 16 * (r + 1))
                main = SHIFTS * SPAN
                nc.vector.tensor_tensor_reduce(
                    out=weighted[:, 0:main].rearrange("p (d i) -> p d i", i=SPAN),
                    in0=weight[:, 0:main].rearrange("p (d i) -> p d i", i=SPAN),
                    in1=window_view(gram, 1, [[1, SHIFTS], [FIELDS + 1, SPAN]]),
                    scale=1.0, scalar=0.0, op0=ALU.mult, op1=ALU.add,
                    accum_out=round_stats[:, 2:3]).then_inc(sums_done, 1)
                for half in range(2):
                    rows = slice(half * P // 2, (half + 1) * P // 2)
                    nc.vector.tensor_tensor_reduce(
                        out=weighted[rows, main:HALF], in0=weight[rows, main:HALF],
                        in1=window_view(gram, SPAN + half * LAST * (FIELDS + 1), [[FIELDS + 1, LAST]], rows),
                        scale=1.0, scalar=0.0, op0=ALU.mult, op1=ALU.add,
                        accum_out=round_stats[rows, 3:4]).then_inc(sums_done, 1)
                dve.wait_ge(sums_done, 3 * (r + 1))
                nc.vector.tensor_copy(stats[:, :, bass.ds(r, 1)],
                                      round_stats[:, :].rearrange("p (n o) -> p n o", o=1)).then_inc(stats_kept, 1)

            def round_steps(r, odd, first=False):
                for t in range(WINDOWS):
                    products(r, t)
                    if t == 0 and first:
                        dve.wait_ge(w1_ready, 1)
                        dve.wait_ge(w1_high_ready, 1)
                        nc.vector.tensor_tensor(w1_low[:, :], w1_block[:, :], w1_high[:, :].bitcast(F32),
                                                ALU.subtract).then_inc(w1_low_ready, 1)
                    if t == MAX_AT and not first:
                        softmax_of_round(r - 1, logit_bank[1 - odd])
                    if t == SUMS_AT and not first:
                        sums_of_round(r - 1)
                    if t >= LOW_LAG and not (first and t - LOW_LAG < LEAD):
                        low_parts(r, t - LOW_LAG)
                    elif t < LOW_LAG and not first:
                        low_parts(r - 1, WINDOWS + t - LOW_LAG)

            dve.memset(w1_rows[:, :], 0.0).then_inc(zeroed, 1)
            dve.memset(w2_window[:, :], 0.0).then_inc(zeroed, 1)
            dve.memset(x_scaled[:, :], 0.0).then_inc(zeroed, 1)
            dve.memset(turn_bank[:, GRAM_AT_COLUMN:GRAM_END], 0.0).then_inc(zeroed, 1)
            round_steps(0, 0, first=True)
            dve.wait_ge(offsets_loaded, 2 * 16)
            with dve.Fori(0, ROUNDS // 2 - 1) as pair:
                round_steps(2 * pair + 1, 1)
                round_steps(2 * pair + 2, 0)
            round_steps(ROUNDS - 1, 1)
            for t in range(WINDOWS - LOW_LAG, WINDOWS):
                low_parts(ROUNDS - 1, t)
            softmax_of_round(ROUNDS - 1, logit_bank[1])
            sums_of_round(ROUNDS - 1)

            dve.wait_ge(stats_turned, 1)
            maximum = turn_bank[0:ROUNDS, 0:P].rearrange("r (h s) -> r h s", h=2)
            sums = turn_bank[0:ROUNDS, P:4 * P].rearrange("r (n hs) -> r n hs", n=3)
            rounds = slice(0, ROUNDS)
            chained = [ROUNDS]

            def chain(instruction):
                chained[0] += 1
                instruction.then_inc(dve_chain, 1)
                dve.wait_ge(dve_chain, chained[0])

            chain(nc.vector.tensor_copy(maxima[:, :, :], maximum))
            chain(nc.vector.tensor_tensor(top[:, :], maxima[:, 0, :], maxima[:, 1, :], ALU.max))
            nc.vector.tensor_tensor(down[:, :, :], maxima[:, :, :],
                                    window_view(top, 0, [[0, 2], [1, P // 2]], rounds),
                                    ALU.subtract).then_inc(down_ready, 1)
            dve.wait_ge(scale_ready, 1)
            chain(nc.vector.tensor_tensor(part[:, :, :], sums, window_view(scale, 0, [[0, 3], [1, P]], rounds),
                                          ALU.mult))
            chain(nc.vector.tensor_tensor(total[:, :, :], part[:, :, 0:P // 2], part[:, :, P // 2:P], ALU.add))
            chain(nc.vector.tensor_tensor(weighted_sum[:, :], total[:, 1, :], total[:, 2, :], ALU.add))
            chain(nc.vector.reciprocal(inverse[:, :], total[:, 0, :]))
            chain(nc.vector.tensor_tensor(ratio[:, :], weighted_sum[:, :], inverse[:, :], ALU.mult))
            nc.vector.tensor_scalar(y_out[:, :].rearrange("r (a k j) -> r j a k", a=2, j=STEP_DUOS),
                                    ratio[:, :].rearrange("r (j a k) -> r j a k", j=STEP_DUOS, a=2),
                                    bl_col[rounds, 0:1], None, ALU.add).then_inc(y_ready, 1)


_INS = ['r_x', 'L0_rec_W1', 'L0_rec_b1', 'L0_rec_W2', 'L0_rec_b2', 'L0_rec_Wl', 'L0_rec_bl']


def kernel(**inputs):
    import numpy as np
    import concourse.bacc as bacc
    from concourse.bass_utils import run_bass_kernel_spmd

    nc = bacc.Bacc("TRN2", target_bir_lowering=False, num_devices=1)
    arrays, args = {}, []
    for name in _INS:
        a = np.ascontiguousarray(inputs[name])
        arrays[f"in_{name}"] = a
        args.append(nc.dram_tensor(f"in_{name}", a.shape, mybir.dt.from_np(a.dtype), kind="ExternalInput").ap())
    y = nc.dram_tensor("out_y", (inputs['r_x'].shape[0], 1), F32, kind="ExternalOutput").ap()
    pair_attention_kernel(nc, *args, y)
    return run_bass_kernel_spmd(nc, [arrays], core_ids=[0]).results[0]["out_y"]
```
